# Optimizing a Trainium2 kernel written in Bass

```python
import numpy as np
import jax
import jax.numpy as jnp

def _softmax(x, axis=-1):
    return jax.nn.softmax(x, axis=axis)

def _gelu(x):
    return jax.nn.gelu(x, approximate=True)

def _silu(x):
    return jax.nn.silu(x)

def _sigmoid(x):
    return jax.nn.sigmoid(x)

def _layernorm(x, axis=-1, eps=1e-05):
    m = jnp.mean(x, axis=axis, keepdims=True)
    v = jnp.var(x, axis=axis, keepdims=True)
    return (x - m) / jnp.sqrt(v + eps)

def _scatter_add(tgt, idx, src, axis=0):
    return tgt.at[idx].add(src)

def _segment_sum(src, seg, n):
    return jax.ops.segment_sum(src, seg, n)
kernel_name = 'mk_rec_standalone_d1_rec_r8_5ec8dd'

def setup_inputs(seed: int=0):
    np.random.seed(seed)
    _w = jnp.asarray

    def _rec_inputs():
        import jax
        import jax.numpy as jnp
        _rk = jax.random.key(seed)
        r_x = -0.000125008 + 0.999885 * jax.random.normal(jax.random.fold_in(_rk, 1), (512, 512), jnp.float32)
        return r_x
    r_x = _rec_inputs()

    def _L0_rec_setup():
        import jax, jax.numpy as jnp
        import numpy as np
        N_DIM = 512
        K_DIM = 256
        BATCH = 1024
        key = jax.random.key(seed)
        k_x, k_v, k_w, k_b = jax.random.split(key, 4)
        x = jax.random.normal(k_x, (BATCH, N_DIM), dtype=jnp.float32)
        V = 0.001 * jax.random.normal(k_v, (N_DIM, K_DIM), dtype=jnp.float32)
        bound = 1.0 / np.sqrt(N_DIM)
        w = jax.random.uniform(k_w, (N_DIM,), dtype=jnp.float32, minval=-bound, maxval=bound)
        b = jax.random.uniform(k_b, (1,), dtype=jnp.float32, minval=-bound, maxval=bound)
        return {'x': x, 'V': V, 'w': w, 'b': b}
    _L0_rec_all = _L0_rec_setup()
    _L0_rec_in = {k: v for k, v in _L0_rec_all.items() if k in ('V', 'w', 'b')}
    del _L0_rec_all
    return {'r_x': r_x, 'L0_rec_V': _L0_rec_in['V'], 'L0_rec_w': _L0_rec_in['w'], 'L0_rec_b': _L0_rec_in['b']}

def reference(r_x, L0_rec_V, L0_rec_w, L0_rec_b):
    import jax
    import jax.numpy as jnp

    def _L0_rec_ref(x, V, w, b):
        import jax, jax.numpy as jnp
        import numpy as np
        N_DIM = 512
        K_DIM = 256
        BATCH = 1024
        linear_outs = x @ w[:, None] + b
        v_v = V @ V.T
        xm = x @ v_v
        interaction = jnp.sum(xm * x, axis=1, keepdims=True)
        return linear_outs + interaction
    y = _L0_rec_ref(r_x, L0_rec_V, L0_rec_w, L0_rec_b)
    return y

_drawn_inputs = setup_inputs


def setup_inputs(seed=0):
    import zlib

    import numpy as np

    out = dict(_drawn_inputs(seed))
    spreads = {}
    factors = {'L0_rec_V': 2.972}
    for name, (base, spread) in spreads.items():
        noise = np.random.default_rng([zlib.crc32(name.encode()), seed]).standard_normal(out[name].shape)
        drawn = base * np.exp(spread * noise) if base else spread * noise
        out[name] = jnp.asarray(drawn.astype(out[name].dtype))
    for name, factor in factors.items():
        out[name] = (out[name] * factor).astype(out[name].dtype)
    return out
```

```python
from contextlib import ExitStack

import concourse.bass as bass
from concourse import mybir

P = 128
F32 = mybir.dt.float32
ALU = mybir.AluOpType
ACT = mybir.ActivationFunctionType


def bass_factorization_machine_kernel(nc: bass.Bass, xt: bass.AP, vw: bass.AP, bias: bass.AP, out: bass.AP):
    _, CHUNKS, ROWS = xt.shape
    WIDE = vw.shape[2]
    RANK = WIDE - 1
    TILES = ROWS // P

    with ExitStack() as ctx:
        def sb(name, shape):
            return ctx.enter_context(nc.sbuf_tensor(name, shape, F32))

        def sem(name):
            return ctx.enter_context(nc.semaphore(name))

        xt_sb = sb("xt_sb", [P, CHUNKS, ROWS])
        vw_sb = sb("vw_sb", [P, CHUNKS, WIDE])
        bias_sb = sb("bias_sb", [P, 1])
        squares = sb("squares", [P, TILES, RANK])
        sums = sb("sums", [P, TILES])
        result = sb("result", [P, TILES])
        warm = sb("warm", [P, 1])
        proj = [ctx.enter_context(nc.psum_tensor(f"proj{t}", [P, 512], F32)) for t in range(TILES)]

        xt_in = [sem(f"xt_in{c}") for c in range(CHUNKS)]
        vw_in = [sem(f"vw_in{c}") for c in range(CHUNKS)]
        bias_in = sem("bias_in")
        warm_set = sem("warm_set")
        tile_projected = sem("tile_projected")
        tile_squared = sem("tile_squared")
        tile_added = sem("tile_added")
        stored = sem("stored")
        block = ctx.enter_context(nc.Block())

        @block.sync
        def _(sp):
            for c in range(CHUNKS):
                sp.dma_start(xt_sb[:, c, :], xt[:, c, :]).then_inc(xt_in[c], 16)
            sp.wait_ge(tile_added, TILES)
            sp.dma_start(out, result[:, :]).then_inc(stored, 16)
            sp.wait_ge(stored, 16)

        @block.scalar
        def _(act):
            for c in range(CHUNKS):
                act.dma_start(vw_sb[:, c, :], vw[:, c, :]).then_inc(vw_in[c], 16)
            act.dma_start(bias_sb[:, :], bias).then_inc(bias_in, 16)
            act.wait_ge(warm_set, 1)
            nc.scalar.activation(warm[:, :], warm[:, :], ACT.Square)
            for t in range(TILES):
                act.wait_ge(tile_projected, t + 1)
                nc.scalar.activation(squares[:, t, :], proj[t][:, 0:RANK], ACT.Square,
                                     accum_out=sums[:, t:t + 1]).then_inc(tile_squared, 1)

        @block.tensor
        def _(pe):
            for c in range(CHUNKS):
                pe.wait_ge(vw_in[c], 16)
                pe.wait_ge(xt_in[c], 16)
                for t in range(TILES):
                    mm = nc.tensor.matmul(proj[t][:, 0:WIDE], xt_sb[:, c, t * P:(t + 1) * P], vw_sb[:, c, :],
                                          start=(c == 0), stop=(c == CHUNKS - 1))
                    if c == CHUNKS - 1:
                        mm.then_inc(tile_projected, 1)

        @block.vector
        def _(dve):
            nc.vector.memset(warm[:, :], 0.0).then_inc(warm_set, 1)
            dve.wait_ge(bias_in, 16)
            for t in range(TILES):
                dve.wait_ge(tile_squared, t + 1)
                nc.vector.scalar_tensor_tensor(out=result[:, t:t + 1], in0=proj[t][:, RANK:WIDE],
                                               scalar=bias_sb[:, 0:1], in1=sums[:, t:t + 1],
                                               op0=ALU.add, op1=ALU.add).then_inc(tile_added, 1)


def kernel(r_x, L0_rec_V, L0_rec_w, L0_rec_b):
    import numpy as np
    import concourse.bacc as bacc
    from concourse.bass_utils import run_bass_kernel_spmd

    x, V, w, b = (np.ascontiguousarray(a) for a in (r_x, L0_rec_V, L0_rec_w, L0_rec_b))
    rows, n = x.shape
    tiles, chunks = rows // P, n // P
    xt = np.ascontiguousarray(x.reshape(P, tiles, chunks, P).transpose(3, 2, 1, 0).reshape(P, chunks, rows))
    vw = np.concatenate([V, w[:, None]], axis=1)
    vw = np.ascontiguousarray(vw.reshape(chunks, P, -1).transpose(1, 0, 2))
    bias = np.ascontiguousarray(np.broadcast_to(b[None, :], (P, 1)))

    nc = bacc.Bacc("TRN2", target_bir_lowering=False, num_devices=1)
    arrays = {"xt": xt, "vw": vw, "bias": bias}
    aps = [nc.dram_tensor(k, a.shape, F32, kind="ExternalInput").ap() for k, a in arrays.items()]
    out = nc.dram_tensor("out", (P, tiles), F32, kind="ExternalOutput").ap()
    bass_factorization_machine_kernel(nc, *aps, out)
    r = run_bass_kernel_spmd(nc, [arrays], core_ids=[0])
    return r.results[0]["out"].reshape(rows, 1)
```

```python
from contextlib import ExitStack

import concourse.bass as bass
from concourse import mybir

P = 128
F32 = mybir.dt.float32
BF16 = mybir.dt.bfloat16
ALU = mybir.AluOpType
ACT = mybir.ActivationFunctionType

WARM_STEPS = 6
WARM_WIDE = 512


def bass_factorization_machine_kernel(nc: bass.Bass, packed: bass.AP, out: bass.AP, wide: int):
    _, CHUNKS, LINE = packed.shape
    LINEAR = wide - 2
    BIAS = wide - 1
    TILES = (LINE - wide) // P
    HEAD = wide + P

    with ExitStack() as ctx:
        def sb(name, shape, dt=F32):
            return ctx.enter_context(nc.sbuf_tensor(name, shape, dt))

        def sem(name):
            return ctx.enter_context(nc.semaphore(name))

        lines = sb("lines", [P, CHUNKS, LINE])
        squares = sb("squares", [P, TILES, LINEAR])
        sums = sb("sums", [P, TILES])
        result = sb("result", [P, TILES])
        warm_act = sb("warm_act", [P, 1])
        proj = [ctx.enter_context(nc.psum_tensor(f"proj{t}", [P, 512], F32)) for t in range(TILES)]
        ones = nc.const_aps.tensor(1.0, (P, WARM_WIDE), BF16)
        warm_out = ctx.enter_context(nc.psum_tensor("warm_out", [P, 512], F32))

        head_in = sem("head_in")
        rest_in = sem("rest_in")
        chunk_in = [None] + [sem(f"chunk_in{c}") for c in range(1, CHUNKS)]
        warm_set = sem("warm_set")
        tile_projected = sem("tile_projected")
        tile_squared = sem("tile_squared")
        tile_added = sem("tile_added")
        stored = sem("stored")
        block = ctx.enter_context(nc.Block())

        @block.sync
        def _(sp):
            sp.dma_start(lines[:, 0, 0:HEAD], packed[:, 0, 0:HEAD]).then_inc(head_in, 16)
            for c in range(1, CHUNKS, 2):
                sp.dma_start(lines[:, c, :], packed[:, c, :]).then_inc(chunk_in[c], 16)
            sp.wait_ge(tile_added, TILES)
            sp.dma_start(out, result[:, :]).then_inc(stored, 16)
            sp.wait_ge(stored, 16)

        @block.scalar
        def _(act):
            act.dma_start(lines[:, 0, HEAD:LINE], packed[:, 0, HEAD:LINE]).then_inc(rest_in, 16)
            for c in range(2, CHUNKS, 2):
                act.dma_start(lines[:, c, :], packed[:, c, :]).then_inc(chunk_in[c], 16)
            act.wait_ge(warm_set, 1)
            nc.scalar.activation(warm_act[:, :], warm_act[:, :], ACT.Square)
            for t in range(TILES):
                act.wait_ge(tile_projected, t + 1)
                nc.scalar.activation(squares[:, t, :], proj[t][:, 0:LINEAR], ACT.Square,
                                     accum_out=sums[:, t:t + 1]).then_inc(tile_squared, 1)

        @block.tensor
        def _(pe):
            for _ in range(WARM_STEPS):
                nc.tensor.matmul(warm_out[:, 0:WARM_WIDE], ones[:, 0:P], ones, start=True, stop=True)
            for c in range(CHUNKS):
                if c > 0:
                    pe.wait_ge(chunk_in[c], 16)
                for t in range(TILES):
                    if c == 0 and t == 0:
                        pe.wait_ge(head_in, 16)
                    if c == 0 and t == 1:
                        pe.wait_ge(rest_in, 16)
                    mm = nc.tensor.matmul(proj[t][:, 0:wide - 1],
                                          lines[:, c, wide + t * P:wide + (t + 1) * P],
                                          lines[:, c, 0:wide - 1], start=(c == 0), stop=(c == CHUNKS - 1))
                    if c == CHUNKS - 1:
                        mm.then_inc(tile_projected, 1)

        @block.vector
        def _(dve):
            nc.vector.memset(warm_act[:, :], 1.0).then_inc(warm_set, 1)
            dve.wait_ge(head_in, 16)
            for t in range(TILES):
                dve.wait_ge(tile_squared, t + 1)
                nc.vector.scalar_tensor_tensor(out=result[:, t:t + 1], in0=proj[t][:, LINEAR:LINEAR + 1],
                                               scalar=lines[:, 0, BIAS:BIAS + 1], in1=sums[:, t:t + 1],
                                               op0=ALU.add, op1=ALU.add).then_inc(tile_added, 1)


def kernel(r_x, L0_rec_V, L0_rec_w, L0_rec_b):
    import numpy as np
    import concourse.bacc as bacc
    from concourse.bass_utils import run_bass_kernel_spmd

    x, V, w, b = (np.ascontiguousarray(a) for a in (r_x, L0_rec_V, L0_rec_w, L0_rec_b))
    rows, n = x.shape
    tiles, chunks = rows // P, n // P
    xt = x.reshape(P, tiles, n).transpose(2, 1, 0).reshape(n, rows)
    packed = np.concatenate([V, w[:, None], np.broadcast_to(b[None, :], (n, 1)), xt], axis=1)
    packed = np.ascontiguousarray(packed.reshape(chunks, P, -1).transpose(1, 0, 2))

    nc = bacc.Bacc("TRN2", target_bir_lowering=False, num_devices=1)
    packed_in = nc.dram_tensor("packed", packed.shape, F32, kind="ExternalInput").ap()
    out = nc.dram_tensor("out", (P, tiles), F32, kind="ExternalOutput").ap()
    bass_factorization_machine_kernel(nc, packed_in, out, V.shape[1] + 2)
    r = run_bass_kernel_spmd(nc, [{"packed": packed}], core_ids=[0])
    return r.results[0]["out"].reshape(rows, 1)
```

```python
from contextlib import ExitStack

import concourse.bass as bass
from concourse import mybir

P = 128
F32 = mybir.dt.float32
F32R = mybir.dt.float32r
BF16 = mybir.dt.bfloat16
ALU = mybir.AluOpType
ACT = mybir.ActivationFunctionType

DIRECT = (2, 1, 0, 0)
DVE_HI = (4, 4, 2, 0)
DVE_SQUARED = 1
BANK = 512
WARM_STEPS = 6


def line_layout(c, t, tiles, wide):
    chunk = c * (wide + tiles * P)
    return chunk, chunk + wide + t * P


def bass_factorization_machine_kernel(nc: bass.Bass, packed: bass.AP, out: bass.AP, chunks: int, wide: int):
    LINEAR = wide - 2
    BIAS = wide - 1
    TILES = out.shape[1]
    LINE = packed.shape[1]
    LAST = chunks - 1

    def v_at(c):
        return line_layout(c, 0, TILES, wide)[0]

    def x_at(c, t):
        return line_layout(c, t, TILES, wide)[1]

    loads = [(v_at(0), x_at(0, 1)), (x_at(0, 1), v_at(1))]
    loads += [(v_at(c), v_at(c + 1)) for c in range(1, chunks)]

    act_hi, dve_hi, los = [], [], []
    for c in range(chunks):
        v_part = (v_at(c), x_at(c, 0))
        act_hi.append(v_part)
        if DVE_HI[c] > 0:
            x_part = (x_at(c, DIRECT[c]), x_at(c, DVE_HI[c]))
            dve_hi.append(x_part)
            los.append(x_part)
        los.append(v_part)
        for t in range(DVE_HI[c], TILES, 2):
            x_part = (x_at(c, t), x_at(c, t + 2))
            act_hi.append(x_part)
            los.append(x_part)

    def count(parts, at):
        return next((i + 1 for i, (a, b) in enumerate(parts) if a <= at < b), 0)

    with ExitStack() as ctx:
        def sb(name, shape, dt=F32):
            return ctx.enter_context(nc.sbuf_tensor(name, shape, dt))

        def sem(name):
            return ctx.enter_context(nc.semaphore(name))

        line = sb("line", [P, LINE])
        hi = sb("hi", [P, LINE], F32R)
        lo = sb("lo", [P, LINE], F32R)
        squares = sb("squares", [P, TILES, LINEAR])
        copied = sb("copied", [P, LINEAR])
        sums = sb("sums", [P, TILES])
        result = sb("result", [P, TILES])
        warm_act = sb("warm_act", [P, 1])
        proj = ctx.enter_context(nc.psum_tensor("proj", [P, TILES, BANK], F32))
        ones = nc.const_aps.tensor(1.0, (P, BANK), BF16)
        warm_out = ctx.enter_context(nc.psum_tensor("warm_out", [P, BANK], F32))

        loaded = [sem(f"loaded{i}") for i in range(len(loads))]
        warm_set = sem("warm_set")
        act_hi_ready = sem("act_hi_ready")
        dve_hi_ready = sem("dve_hi_ready")
        lo_ready = sem("lo_ready")
        tile_projected = sem("tile_projected")
        act_squared = sem("act_squared")
        tile_copied = sem("tile_copied")
        dve_squared = sem("dve_squared")
        added = sem("added")
        stored = sem("stored")
        block = ctx.enter_context(nc.Block())

        def wait_hi(engine, at):
            if count(act_hi, at):
                engine.wait_ge(act_hi_ready, count(act_hi, at))
            else:
                engine.wait_ge(dve_hi_ready, count(dve_hi, at))

        @block.sync
        def _(sp):
            for i, (a, b) in enumerate(loads):
                sp.dma_start(line[:, a:b], packed[:, a:b]).then_inc(loaded[i], 16)
            sp.wait_ge(added, 1)
            sp.dma_start(out, result[:, :]).then_inc(stored, 16)
            sp.wait_ge(stored, 16)

        @block.scalar
        def _(act):
            act.wait_ge(warm_set, 1)
            nc.scalar.activation(warm_act[:, :], warm_act[:, :], ACT.Square)
            for a, b in act_hi:
                act.wait_ge(loaded[count(loads, a) - 1], 16)
                nc.scalar.copy(hi[:, a:b], line[:, a:b]).then_inc(act_hi_ready, 1)
            for t in range(TILES):
                if t == DVE_SQUARED:
                    continue
                act.wait_ge(tile_projected, t + 1)
                nc.scalar.activation(squares[:, t, :], proj[:, t, 0:LINEAR], ACT.Square,
                                     accum_out=sums[:, t:t + 1]).then_inc(act_squared, 1)

        @block.vector
        def _(dve):
            nc.vector.memset(warm_act[:, :], 1.0).then_inc(warm_set, 1)

            for a, b in los:
                if (a, b) in dve_hi:
                    dve.wait_ge(loaded[count(loads, a) - 1], 16)
                    nc.vector.tensor_copy(hi[:, a:b], line[:, a:b]).then_inc(dve_hi_ready, 1)
                wait_hi(dve, a)
                nc.vector.tensor_tensor(lo[:, a:b], line[:, a:b], hi[:, a:b].bitcast(F32),
                                        ALU.subtract).then_inc(lo_ready, 1)

            t = DVE_SQUARED
            dve.wait_ge(tile_projected, t + 1)
            nc.vector.tensor_copy(copied[:, :], proj[:, t, 0:LINEAR]).then_inc(tile_copied, 1)
            dve.wait_ge(tile_copied, 1)
            nc.vector.tensor_tensor_reduce(squares[:, t, :], proj[:, t, 0:LINEAR], copied[:, :], 1.0, 0.0,
                                           ALU.mult, ALU.add, sums[:, t:t + 1]).then_inc(dve_squared, 1)
            dve.wait_ge(act_squared, TILES - 1)
            dve.wait_ge(dve_squared, 1)
            nc.vector.scalar_tensor_tensor(out=result[:, :], in0=proj[:, :, LINEAR], scalar=line[:, BIAS:BIAS + 1],
                                           in1=sums[:, :], op0=ALU.add, op1=ALU.add).then_inc(added, 1)

        @block.tensor
        def _(pe):
            def project(c, t, x_part, v_part, first=False, last=False):
                x, v = x_at(c, t), v_at(c)
                return nc.tensor.matmul(proj[:, t, 0:wide], x_part[:, x:x + P], v_part[:, v:v + wide],
                                        start=first, stop=last)

            def wait_lo(at):
                pe.wait_ge(lo_ready, count(los, at))

            for _ in range(WARM_STEPS):
                nc.tensor.matmul(warm_out[:, :], ones[:, 0:P], ones, start=True, stop=True)

            for c in range(LAST):
                for t in range(DIRECT[c]):
                    pe.wait_ge(loaded[count(loads, x_at(c, t)) - 1], 16)
                    project(c, t, line, line, first=(c == 0))
                wait_hi(pe, v_at(c))
                for t in range(DIRECT[c], TILES):
                    if t in (DIRECT[c], DVE_HI[c]):
                        wait_hi(pe, x_at(c, t))
                    project(c, t, hi, hi, first=(c == 0))
                wait_lo(x_at(c, DIRECT[c]))
                for t in range(DIRECT[c], DVE_HI[c]):
                    project(c, t, lo, hi)
                wait_lo(v_at(c))
                for t in range(DIRECT[c], TILES):
                    project(c, t, hi, lo)
                for t in range(DVE_HI[c], TILES):
                    if t == DVE_HI[c]:
                        wait_lo(x_at(c, t))
                    project(c, t, lo, hi)

            wait_hi(pe, v_at(LAST))
            wait_hi(pe, x_at(LAST, 0))
            project(LAST, 0, hi, hi)
            project(LAST, 1, hi, hi)
            wait_lo(v_at(LAST))
            project(LAST, 0, hi, lo)
            project(LAST, 1, hi, lo)
            wait_lo(x_at(LAST, 0))
            project(LAST, 0, lo, hi, last=True).then_inc(tile_projected, 1)
            project(LAST, 1, lo, hi, last=True).then_inc(tile_projected, 1)
            wait_hi(pe, x_at(LAST, 2))
            for t in range(2, TILES):
                project(LAST, t, hi, hi)
                project(LAST, t, hi, lo)
                if t == 2:
                    wait_lo(x_at(LAST, t))
                project(LAST, t, lo, hi, last=True).then_inc(tile_projected, 1)


def kernel(r_x, L0_rec_V, L0_rec_w, L0_rec_b):
    import numpy as np
    import concourse.bacc as bacc
    from concourse.bass_utils import run_bass_kernel_spmd

    x, V, w, b = (np.ascontiguousarray(a) for a in (r_x, L0_rec_V, L0_rec_w, L0_rec_b))
    rows, n = x.shape
    tiles, chunks, wide = rows // P, n // P, V.shape[1] + 2
    xt = x.reshape(P, tiles, chunks, P).transpose(3, 2, 1, 0)
    vwb = np.concatenate([V, w[:, None], np.broadcast_to(b[None, :], (n, 1))], axis=1)
    packed = np.empty((P, line_layout(chunks, 0, tiles, wide)[0]), x.dtype)
    for c in range(chunks):
        for t in range(tiles):
            v_at, x_at = line_layout(c, t, tiles, wide)
            packed[:, x_at:x_at + P] = xt[:, c, t]
        packed[:, v_at:v_at + wide] = vwb[c * P:(c + 1) * P]

    nc = bacc.Bacc("TRN2", target_bir_lowering=False, num_devices=1)
    packed_in = nc.dram_tensor("packed", packed.shape, F32, kind="ExternalInput").ap()
    out = nc.dram_tensor("out", (P, tiles), F32, kind="ExternalOutput").ap()
    bass_factorization_machine_kernel(nc, packed_in, out, chunks, wide)
    r = run_bass_kernel_spmd(nc, [{"packed": packed}], core_ids=[0])
    return r.results[0]["out"].reshape(rows, 1)
```
